# Optimizing a Trainium2 kernel written in Bass

```python
import numpy as np
import jax
import jax.numpy as jnp

def _softmax(x, axis=-1):
    return jax.nn.softmax(x, axis=axis)

def _gelu(x):
    return jax.nn.gelu(x, approximate=True)

def _silu(x):
    return jax.nn.silu(x)

def _sigmoid(x):
    return jax.nn.sigmoid(x)

def _layernorm(x, axis=-1, eps=1e-05):
    m = jnp.mean(x, axis=axis, keepdims=True)
    v = jnp.var(x, axis=axis, keepdims=True)
    return (x - m) / jnp.sqrt(v + eps)

def _scatter_add(tgt, idx, src, axis=0):
    return tgt.at[idx].add(src)

def _segment_sum(src, seg, n):
    return jax.ops.segment_sum(src, seg, n)
kernel_name = 'mk_pixart_seq_d2_seqx_r4_369de7'

def setup_inputs(seed: int=0):
    np.random.seed(seed)
    _w = jnp.asarray

    def _rec_inputs():
        import jax
        import jax.numpy as jnp
        _rk = jax.random.key(seed)
        x = -0.0003929 + 0.9999 * jax.random.normal(jax.random.fold_in(_rk, 1), (64, 128, 256), jnp.float32)
        _lenS = 128 - jax.random.randint(jax.random.fold_in(_rk, 7), (64,), 0, max(1, 128 // 4) + 1, jnp.int32)
        _lenS2 = 128 - jax.random.randint(jax.random.fold_in(_rk, 8), (64,), 0, max(1, 128 // 4) + 1, jnp.int32)
        _ctx_1024P = jax.random.normal(jax.random.fold_in(_rk, 11), (64, 16, 256), jnp.float32)
        _ctx_1024c = jax.random.dirichlet(jax.random.fold_in(_rk, 511), 0.3 * jnp.ones((16,), jnp.float32), (64, 128))
        _ctx_1024t = jnp.einsum('bsk,bkd->bsd', _ctx_1024c, _ctx_1024P)
        _ctx_1024t = _ctx_1024t * jax.lax.rsqrt(jnp.mean(jnp.square(_ctx_1024t)) + 1e-12) * 0.953939
        ctx_1024 = -1.39393e-06 + 0.999914 * (_ctx_1024t + 0.3 * jax.random.normal(jax.random.fold_in(_rk, 611), (64, 128, 256), jnp.float32))
        cond_1024 = -0.00920427 + 1.00102 * jax.random.normal(jax.random.fold_in(_rk, 12), (64, 256), jnp.float32)
        return (x, ctx_1024, cond_1024)
    x, ctx_1024, cond_1024 = _rec_inputs()

    def _L0_xcond_setup():
        import jax, jax.numpy as jnp
        import numpy as np
        EPS = 1e-05

        def _ada_ln(x, c, W_ss, b_ss):
            mu = jnp.mean(x, axis=-1, keepdims=True)
            var = jnp.mean((x - mu) ** 2, axis=-1, keepdims=True)
            h = (x - mu) / jnp.sqrt(var + EPS)
            ss = jax.nn.silu(c) @ W_ss + b_ss
            scale, bias = jnp.split(ss, 2, axis=-1)
            return (1.0 + scale)[:, None, :] * h + bias[:, None, :]
        key = jax.random.key(seed)
        ks = jax.random.split(key, 12)
        B, Lq, Lkv, H = (8, 512, 128, 256)
        s = 0.02
        return {'x_q': jax.random.normal(ks[0], (B, Lq, H), jnp.float32), 'x_kv': jax.random.normal(ks[1], (B, Lkv, H), jnp.float32), 't_vec': jax.random.normal(ks[2], (B, H), jnp.float32), 'Wq': jax.random.normal(ks[3], (H, H), jnp.float32) * s, 'bq': jnp.zeros((H,), jnp.float32), 'Wkv': jax.random.normal(ks[4], (H, 2 * H), jnp.float32) * s, 'bkv': jnp.zeros((2 * H,), jnp.float32), 'Wp': jax.random.normal(ks[5], (H, H), jnp.float32) * s, 'bp': jnp.zeros((H,), jnp.float32), 'Wss_q': jax.random.normal(ks[6], (H, 2 * H), jnp.float32) * s, 'bss_q': jnp.zeros((2 * H,), jnp.float32), 'Wss_kv': jax.random.normal(ks[7], (H, 2 * H), jnp.float32) * s, 'bss_kv': jnp.zeros((2 * H,), jnp.float32)}
    _L0_xcond_all = _L0_xcond_setup()
    _L0_xcond_in = {k: v for k, v in _L0_xcond_all.items() if k in ('Wq', 'bq', 'Wkv', 'bkv', 'Wp', 'bp', 'Wss_q', 'bss_q', 'Wss_kv', 'bss_kv')}
    del _L0_xcond_all

    def _L1_xcond_setup():
        import jax, jax.numpy as jnp
        import numpy as np
        D = 256
        H = 16
        HD = D // H
        MLP = 4 * D
        EPS = 1e-06
        SCALE = HD ** (-0.5)

        def _p(key, shape, s=0.02):
            return jax.random.normal(key, shape, dtype=jnp.float32) * s

        def _ln(x):
            mu = jnp.mean(x, axis=-1, keepdims=True)
            var = jnp.var(x, axis=-1, keepdims=True)
            return (x - mu) * jax.lax.rsqrt(var + EPS)

        def _heads(t):
            B, L, _ = t.shape
            return t.reshape(B, L, H, HD).transpose(0, 2, 1, 3)

        def _attend(q, k, v):
            attn = jnp.einsum('bhnd,bhsd->bhns', q, k) * SCALE
            attn = jax.nn.softmax(attn, axis=-1)
            o = jnp.einsum('bhns,bhsd->bhnd', attn, v)
            B, _, N, _ = q.shape
            return o.transpose(0, 2, 1, 3).reshape(B, N, D)
        key = jax.random.key(seed)
        ks = jax.random.split(key, 24)
        B, N, S = (4, 256, 77)
        return {'x': jax.random.normal(ks[0], (B, N, D), dtype=jnp.float32), 't_emb': jax.random.normal(ks[1], (B, D), dtype=jnp.float32), 'context': jax.random.normal(ks[2], (B, S, D), dtype=jnp.float32), 'adaln_w': _p(ks[3], (D, 6 * D)), 'adaln_b': _p(ks[4], (6 * D,)), 'qkv_w': _p(ks[5], (D, 3 * D)), 'qkv_b': _p(ks[6], (3 * D,)), 'sa_proj_w': _p(ks[7], (D, D)), 'sa_proj_b': _p(ks[8], (D,)), 'q_w': _p(ks[9], (D, D)), 'q_b': _p(ks[10], (D,)), 'kv_w': _p(ks[11], (D, 2 * D)), 'kv_b': _p(ks[12], (2 * D,)), 'ca_proj_w': _p(ks[13], (D, D)), 'ca_proj_b': _p(ks[14], (D,)), 'fc1_w': _p(ks[15], (D, MLP)), 'fc1_b': _p(ks[16], (MLP,)), 'fc2_w': _p(ks[17], (MLP, D)), 'fc2_b': _p(ks[18], (D,))}
    _L1_xcond_all = _L1_xcond_setup()
    _L1_xcond_in = {k: v for k, v in _L1_xcond_all.items() if k in ('adaln_w', 'adaln_b', 'qkv_w', 'qkv_b', 'sa_proj_w', 'sa_proj_b', 'q_w', 'q_b', 'kv_w', 'kv_b', 'ca_proj_w', 'ca_proj_b', 'fc1_w', 'fc1_b', 'fc2_w', 'fc2_b')}
    del _L1_xcond_all
    return {'x': x, 'ctx_1024': ctx_1024, 'cond_1024': cond_1024, 'L0_xcond_Wq': _L0_xcond_in['Wq'], 'L0_xcond_bq': _L0_xcond_in['bq'], 'L0_xcond_Wkv': _L0_xcond_in['Wkv'], 'L0_xcond_bkv': _L0_xcond_in['bkv'], 'L0_xcond_Wp': _L0_xcond_in['Wp'], 'L0_xcond_bp': _L0_xcond_in['bp'], 'L0_xcond_Wss_q': _L0_xcond_in['Wss_q'], 'L0_xcond_bss_q': _L0_xcond_in['bss_q'], 'L0_xcond_Wss_kv': _L0_xcond_in['Wss_kv'], 'L0_xcond_bss_kv': _L0_xcond_in['bss_kv'], 'L1_xcond_adaln_w': _L1_xcond_in['adaln_w'], 'L1_xcond_adaln_b': _L1_xcond_in['adaln_b'], 'L1_xcond_qkv_w': _L1_xcond_in['qkv_w'], 'L1_xcond_qkv_b': _L1_xcond_in['qkv_b'], 'L1_xcond_sa_proj_w': _L1_xcond_in['sa_proj_w'], 'L1_xcond_sa_proj_b': _L1_xcond_in['sa_proj_b'], 'L1_xcond_q_w': _L1_xcond_in['q_w'], 'L1_xcond_q_b': _L1_xcond_in['q_b'], 'L1_xcond_kv_w': _L1_xcond_in['kv_w'], 'L1_xcond_kv_b': _L1_xcond_in['kv_b'], 'L1_xcond_ca_proj_w': _L1_xcond_in['ca_proj_w'], 'L1_xcond_ca_proj_b': _L1_xcond_in['ca_proj_b'], 'L1_xcond_fc1_w': _L1_xcond_in['fc1_w'], 'L1_xcond_fc1_b': _L1_xcond_in['fc1_b'], 'L1_xcond_fc2_w': _L1_xcond_in['fc2_w'], 'L1_xcond_fc2_b': _L1_xcond_in['fc2_b']}

def reference(x, ctx_1024, cond_1024, L0_xcond_Wq, L0_xcond_bq, L0_xcond_Wkv, L0_xcond_bkv, L0_xcond_Wp, L0_xcond_bp, L0_xcond_Wss_q, L0_xcond_bss_q, L0_xcond_Wss_kv, L0_xcond_bss_kv, L1_xcond_adaln_w, L1_xcond_adaln_b, L1_xcond_qkv_w, L1_xcond_qkv_b, L1_xcond_sa_proj_w, L1_xcond_sa_proj_b, L1_xcond_q_w, L1_xcond_q_b, L1_xcond_kv_w, L1_xcond_kv_b, L1_xcond_ca_proj_w, L1_xcond_ca_proj_b, L1_xcond_fc1_w, L1_xcond_fc1_b, L1_xcond_fc2_w, L1_xcond_fc2_b):
    import jax
    import jax.numpy as jnp

    def _L0_xcond_ref(x_q, x_kv, t_vec, Wq, bq, Wkv, bkv, Wp, bp, Wss_q, bss_q, Wss_kv, bss_kv):
        import jax, jax.numpy as jnp
        import numpy as np
        EPS = 1e-05

        def _ada_ln(x, c, W_ss, b_ss):
            mu = jnp.mean(x, axis=-1, keepdims=True)
            var = jnp.mean((x - mu) ** 2, axis=-1, keepdims=True)
            h = (x - mu) / jnp.sqrt(var + EPS)
            ss = jax.nn.silu(c) @ W_ss + b_ss
            scale, bias = jnp.split(ss, 2, axis=-1)
            return (1.0 + scale)[:, None, :] * h + bias[:, None, :]
        B, Lq, H = x_q.shape
        Lkv = x_kv.shape[1]
        nh = 16
        dh = H // nh
        xq = _ada_ln(x_q, t_vec, Wss_q, bss_q)
        xkv = _ada_ln(x_kv, t_vec, Wss_kv, bss_kv)
        q = (xq @ Wq + bq).reshape(B, Lq, nh, dh)
        kv = (xkv @ Wkv + bkv).reshape(B, Lkv, 2, nh, dh)
        k = kv[:, :, 0]
        v = kv[:, :, 1]
        scores = jnp.einsum('bqhd,bkhd->bhqk', q, k) / jnp.sqrt(jnp.float32(dh))
        attn = jax.nn.softmax(scores, axis=-1)
        out = jnp.einsum('bhqk,bkhd->bqhd', attn, v).reshape(B, Lq, H)
        return x_q + (out @ Wp + bp)

    def _L1_xcond_ref(x, t_emb, context, adaln_w, adaln_b, qkv_w, qkv_b, sa_proj_w, sa_proj_b, q_w, q_b, kv_w, kv_b, ca_proj_w, ca_proj_b, fc1_w, fc1_b, fc2_w, fc2_b):
        import jax, jax.numpy as jnp
        import numpy as np
        D = 256
        H = 16
        HD = D // H
        MLP = 4 * D
        EPS = 1e-06
        SCALE = HD ** (-0.5)

        def _p(key, shape, s=0.02):
            return jax.random.normal(key, shape, dtype=jnp.float32) * s

        def _ln(x):
            mu = jnp.mean(x, axis=-1, keepdims=True)
            var = jnp.var(x, axis=-1, keepdims=True)
            return (x - mu) * jax.lax.rsqrt(var + EPS)

        def _heads(t):
            B, L, _ = t.shape
            return t.reshape(B, L, H, HD).transpose(0, 2, 1, 3)

        def _attend(q, k, v):
            attn = jnp.einsum('bhnd,bhsd->bhns', q, k) * SCALE
            attn = jax.nn.softmax(attn, axis=-1)
            o = jnp.einsum('bhns,bhsd->bhnd', attn, v)
            B, _, N, _ = q.shape
            return o.transpose(0, 2, 1, 3).reshape(B, N, D)
        B, N, _ = x.shape
        S = context.shape[1]
        mod = jax.nn.silu(t_emb) @ adaln_w + adaln_b
        sh_sa, sc_sa, g_sa, sh_ff, sc_ff, g_ff = jnp.split(mod[:, None, :], 6, axis=-1)
        xm = _ln(x) * (1.0 + sc_sa) + sh_sa
        qkv = (xm @ qkv_w + qkv_b).reshape(B, N, 3, H, HD)
        q = qkv[:, :, 0].transpose(0, 2, 1, 3)
        k = qkv[:, :, 1].transpose(0, 2, 1, 3)
        v = qkv[:, :, 2].transpose(0, 2, 1, 3)
        x_sa = _attend(q, k, v) @ sa_proj_w + sa_proj_b
        x = x + g_sa * x_sa
        xn = _ln(x)
        q = _heads(xn @ q_w + q_b)
        kv = (context @ kv_w + kv_b).reshape(B, S, 2, H, HD)
        k = kv[:, :, 0].transpose(0, 2, 1, 3)
        v = kv[:, :, 1].transpose(0, 2, 1, 3)
        x_ca = _attend(q, k, v) @ ca_proj_w + ca_proj_b
        x = x + x_ca
        xm = _ln(x) * (1.0 + sc_ff) + sh_ff
        h = jax.nn.gelu(xm @ fc1_w + fc1_b, approximate=True)
        x_ff = h @ fc2_w + fc2_b
        x = x + g_ff * x_ff
        return x
    x = _L0_xcond_ref(x, ctx_1024, cond_1024, L0_xcond_Wq, L0_xcond_bq, L0_xcond_Wkv, L0_xcond_bkv, L0_xcond_Wp, L0_xcond_bp, L0_xcond_Wss_q, L0_xcond_bss_q, L0_xcond_Wss_kv, L0_xcond_bss_kv)
    x = _L1_xcond_ref(x, cond_1024, ctx_1024, L1_xcond_adaln_w, L1_xcond_adaln_b, L1_xcond_qkv_w, L1_xcond_qkv_b, L1_xcond_sa_proj_w, L1_xcond_sa_proj_b, L1_xcond_q_w, L1_xcond_q_b, L1_xcond_kv_w, L1_xcond_kv_b, L1_xcond_ca_proj_w, L1_xcond_ca_proj_b, L1_xcond_fc1_w, L1_xcond_fc1_b, L1_xcond_fc2_w, L1_xcond_fc2_b)
    return x

_drawn_inputs = setup_inputs


def setup_inputs(seed=0):
    import zlib

    import numpy as np

    out = dict(_drawn_inputs(seed))
    spreads = {'L0_xcond_bq': (0.0, 2.0),
     'L0_xcond_bkv': (0.0, 0.1),
     'L0_xcond_bp': (0.0, 0.1),
     'L0_xcond_bss_q': (0.0, 0.8),
     'L0_xcond_bss_kv': (0.0, 0.669)}
    factors = {'L0_xcond_Wq': 8.0,
     'L0_xcond_Wss_q': 8.0,
     'L1_xcond_adaln_b': 8.0,
     'L1_xcond_qkv_w': 8.0,
     'L1_xcond_qkv_b': 8.0,
     'L1_xcond_sa_proj_w': 8.0,
     'L1_xcond_sa_proj_b': 8.0,
     'L1_xcond_q_w': 44.901,
     'L1_xcond_q_b': 64.0,
     'L1_xcond_kv_b': 8.0,
     'L1_xcond_ca_proj_b': 2.944,
     'L1_xcond_fc1_w': 2.699,
     'L1_xcond_fc1_b': 47.778,
     'L1_xcond_fc2_b': 8.0}
    for name, (base, spread) in spreads.items():
        noise = np.random.default_rng([zlib.crc32(name.encode()), seed]).standard_normal(out[name].shape)
        drawn = base * np.exp(spread * noise) if base else spread * noise
        out[name] = jnp.asarray(drawn.astype(out[name].dtype))
    for name, factor in factors.items():
        out[name] = (out[name] * factor).astype(out[name].dtype)
    return out
```

```python
from contextlib import ExitStack

import concourse.bass as bass
from concourse import mybir

F32 = mybir.dt.float32
F32R = mybir.dt.float32r
BF16 = mybir.dt.bfloat16
ACT = mybir.ActivationFunctionType
ALU = mybir.AluOpType
AX = mybir.AxisListType

P = 128
D = 256
KT = D // P
B = 64
HD = 16
H = D // HD
U = 4
G = 4
MLP = 4 * D
MT = MLP // P
STREAMS = 2
TURNS = B // STREAMS
LAYERS = 3
SCALE = HD ** -0.5

BQ = [0, 2, 4]
BK = [6, 8, 10]
MODB = 12
FC1B = 28
NCOLS = FC1B + MT
RV = [0, 1, 2]
RP0, RSA, RCA, RFC2, RGSA, RGFF = 3, 4, 5, 6, 7, 8
NROWS = 9
M_SCQ, M_BQ, M_SCKV, M_BKV, M_SHSA, M_SCSA, M_SHFF, M_SCFF = range(0, 16, 2)
NMOD = 16
C_ID, C_HEADMASK, C_ONES, C_SEL = 0, 128, 140, 204
NCONST = C_SEL + H


def build(nc, a, out):
    with ExitStack() as ctx:
        ctx.enter_context(nc.allow_non_contiguous_dma(reason="weights, once"))

        def sb(name, shape, dt=F32):
            return ctx.enter_context(nc.sbuf_tensor(name, shape, dt))

        def sem(name):
            return ctx.enter_context(nc.semaphore(name))

        def sems(name, n):
            return [sem(f"{name}{j}") for j in range(n)]

        w_q = [sb(f"w_q{l}", [P, KT, D]) for l in range(3)]
        w_k = [sb(f"w_k{l}", [P, KT, D]) for l in range(3)]
        w_v = [sb(f"w_v{l}", [P, KT, D]) for l in range(3)]
        w_o = [sb(f"w_o{l}", [P, KT, D]) for l in range(3)]
        w_fc1 = sb("w_fc1", [P, KT, MLP])
        w_fc2 = sb("w_fc2", [P, MT, D])
        w_ssq = sb("w_ssq", [P, KT, 2 * D])
        w_sskv = sb("w_sskv", [P, KT, 2 * D])
        w_ada = sb("w_ada", [P, KT, 6 * D])
        cols = sb("cols", [P, NCOLS])
        rows = sb("rows", [P, NROWS, D])
        consts = sb("consts", [P, NCONST])
        ident = consts[:, C_ID:C_ID + P]
        keymask = consts[:, C_HEADMASK:C_HEADMASK + 4]
        querymask = consts[:, C_HEADMASK + 4:C_HEADMASK + 12]
        ones_of = consts[:, C_ONES:C_ONES + 64].rearrange("p (e m) -> p e m", e=2)
        ident_b = sb("ident_b", [P, P], BF16)
        sel = sb("sel", [P, H, P], BF16)
        eps_pow = sb("eps_pow", [P, 3, 2])

        cond = sb("cond", [B, D])
        cond_e = sb("cond_e", [B, D])
        cond_d = sb("cond_d", [B, D])
        cond_r = sb("cond_r", [B, D])
        cond_s = sb("cond_s", [B, D])
        condT = sb("condT", [P, KT, B])
        mod_tab = sb("mod_tab", [P, B, NMOD])
        gates = sb("gates", [B, 4, D])

        def per(name, shape, dt=F32):
            return [sb(f"{name}_{s}", shape, dt) for s in range(STREAMS)]

        x_in = per("x_in", [P, D])
        c_in = per("c_in", [P, D])
        in_stats = per("in_stats", [P, 2, 6])
        in_mv = per("in_mv", [P, 2, 2])
        in_ve = per("in_ve", [P, 2])
        in_rstd = per("in_rstd", [P, 2])
        in_hn = per("in_hn", [P, 2, D])
        in_mod = per("in_mod", [P, NMOD // 2])
        stats = per("stats", [P, 6])
        mv = per("mv", [P, 2])
        ve = per("ve", [P, 1])
        rstd = per("rstd", [P, 1])
        hn = per("hn", [P, D])
        mod = per("mod", [P, NMOD // 2])
        xT = per("xT", [P, KT, P])
        cT = per("cT", [P, KT, P])
        crT = per("crT", [P, KT, P])
        mlpT = per("mlpT", [P, KT, P])
        q32 = per("q32", [P, KT, P])
        qr = per("qr", [P, KT, P], F32R)
        qm = per("qm", [P, KT, 8, P])
        k32 = per("k32", [P, KT, P])
        kr = per("kr", [P, KT, 4, P], F32R)
        v = per("v", [P, 8, 4, HD])
        mx = per("mx", [P, H])
        nm = per("nm", [P, P], BF16)
        mT = per("mT", [P, P], BF16)
        prob = per("prob", [P, H, P])
        rsum = per("rsum", [P, KT, P])
        oT = per("oT", [P, KT, P])
        xres = per("xres", [P, D])
        xb0 = per("xb0", [P, D])
        xb = per("xb", [P, D])
        tmp = per("tmp", [P, D])
        gate = per("gate", [P, 4, D])
        hT = per("hT", [P, MT, P])
        y = per("y", [P, D])

        bank = [ctx.enter_context(nc.psum_tensor(f"bank{j}", [P, 512], F32)) for j in range(8)]
        ps_s, ps_st, ps_o, ps_kv, ps_q = bank[0:2], bank[2:4], bank[4:6], bank[6], bank[7]

        cond_loaded = sem("cond_loaded")
        w_loaded = sem("w_loaded")
        gates_stored = sem("gates_stored")
        setup = sem("setup")
        modtab_ready = sem("modtab_ready")
        xc_loaded = sems("xc_loaded", 2)
        gate_loaded = sems("gate_loaded", 2)
        y_stored = sems("y_stored", 2)
        in_mod_copied = sems("in_mod_copied", 2)
        mod_copied = sems("mod_copied", 2)
        in_stat_done = sems("in_stat_done", 2)
        in_aggr_done = sems("in_aggr_done", 2)
        in_ve_ready = sems("in_ve_ready", 2)
        in_rstd_ready = sems("in_rstd_ready", 2)
        in_h_ready = sems("in_h_ready", 2)
        xb0_ready = sems("xb0_ready", 2)
        t0_done = sems("t0_done", 2)
        tc_done = sems("tc_done", 2)
        t0_copied = sems("t0_copied", 2)
        tc_copied = sems("tc_copied", 2)
        o_gated = sems("o_gated", 2)
        fc1_done = [sems(f"fc1_done{s}_", 2) for s in range(STREAMS)]
        gelu_done = sems("gelu_done", 2)
        fc2_done = sems("fc2_done", 2)
        y_gated = sems("y_gated", 2)
        y_ready = sems("y_ready", 2)
        stat_done = sems("stat_done", 2)
        aggr_done = sems("aggr_done", 2)
        ve_ready = sems("ve_ready", 2)
        rstd_ready = sems("rstd_ready", 2)
        h_ready = sems("h_ready", 2)
        xb_ready = sems("xb_ready", 2)
        t_done = sems("t_done", 2)
        t_copied = sems("t_copied", 2)
        k_done = sems("k_done", 2)
        q_done = sems("q_done", 2)
        k_copied = [sems(f"k_copied{s}_", KT) for s in range(STREAMS)]
        q_copied = sems("q_copied", 2)
        k_rounded = [sems(f"k_rounded{s}_", KT) for s in range(STREAMS)]
        q_rounded = sems("q_rounded", 2)
        q_masked = [sems(f"q_masked{s}_", 2) for s in range(STREAMS)]
        v_done = sems("v_done", 2)
        v_copied = sems("v_copied", 2)
        s_done = [sems(f"s_done{s}_", U) for s in range(STREAMS)]
        max_done = [sems(f"max_done{s}_", U) for s in range(STREAMS)]
        nm_high = sems("nm_high", 2)
        nm_ready = sems("nm_ready", 2)
        mt_done = sems("mt_done", 2)
        mt_ready = sems("mt_ready", 2)
        st_done = [sems(f"st_done{s}_", U) for s in range(STREAMS)]
        exp_done = [sems(f"exp_done{s}_", U) for s in range(STREAMS)]
        sums_done = sems("sums_done", 2)
        av_done = sems("av_done", 2)
        sum_inverted = sems("sum_inverted", 2)
        o_ready = sems("o_ready", 2)
        o_proj = sems("o_proj", 2)
        x_ready = sems("x_ready", 2)

        gates_dram = nc.dram_tensor("gates_scratch", (B, 4 * D), F32, kind="Internal").ap()
        block = ctx.enter_context(nc.Block())

        weight_loads = []
        for l, (wq, wk, wv, wo) in enumerate((
                (a["L0_xcond_Wq"], a["L0_xcond_Wkv"][:, 0:D], a["L0_xcond_Wkv"][:, D:2 * D], a["L0_xcond_Wp"]),
                (a["L1_xcond_qkv_w"][:, 0:D], a["L1_xcond_qkv_w"][:, D:2 * D],
                 a["L1_xcond_qkv_w"][:, 2 * D:3 * D], a["L1_xcond_sa_proj_w"]),
                (a["L1_xcond_q_w"], a["L1_xcond_kv_w"][:, 0:D], a["L1_xcond_kv_w"][:, D:2 * D],
                 a["L1_xcond_ca_proj_w"]))):
            weight_loads += [(w_q[l], wq), (w_k[l], wk), (w_v[l], wv), (w_o[l], wo)]
        weight_loads += [(w_fc1, a["L1_xcond_fc1_w"]), (w_fc2, a["L1_xcond_fc2_w"])]
        cond_weight_loads = [(w_ssq, a["L0_xcond_Wss_q"]), (w_sskv, a["L0_xcond_Wss_kv"]),
                             (w_ada, a["L1_xcond_adaln_w"])]
        N_W = 16 * len(weight_loads)
        N_COND = 16 * (len(cond_weight_loads) + 4)

        def sample(ap, n, s):
            return ap[bass.ds(2 * n + s, 1)].rearrange("b p d -> (b p) d")

        def gates_of(n, s):
            return gates_dram[bass.ds(2 * n + s, 1), :].to_broadcast([P, 4 * D])

        (EXP_COND, COND_PLUS_1, COND_INVERTED, SILU_READY, SILU_TRANSPOSED, SILU_COPIED, MOD_PRODUCTS) = range(1, 8)
        GATES_READY = MOD_PRODUCTS + 2
        ALL_SET = GATES_READY + 2
        TABLES = 7 + NMOD

        class Counts:

            def __init__(self, eng, i):
                self.eng, self.i, self.known = eng, i, {}
                for mult, ks in ((1, (0, 1)), (3, range(-2, 4))):
                    for k in ks:
                        self.at(mult, k)

            def at(self, mult, k):
                if (mult, k) not in self.known:
                    x = mult * self.i + k
                    self.known[mult, k] = x if isinstance(x, int) else self.eng.to_reg(self.eng.snap(x))
                return self.known[mult, k]

            def once(self, old):
                return self.at(1, 1 - old)

            def att(self, l, old):
                return self.at(3, l + 1 - 3 * old)

        def after(eng, sem_, x):
            if not isinstance(x, int) or x > 0:
                eng.wait_ge(sem_, x)

        SLOTS = [(1, 1, 1, 0, 0), (0, 0, 0, 2, 1), (1, 2, 1, 1, 0),
                 (0, 1, 0, 0, 0), (1, 0, 0, 2, 0), (0, 2, 0, 1, 0)]

        def slots(begin, end):
            for x, lx, oldx, ly, oldy in SLOTS:
                yield x, lx if (end if oldx else begin) else None, oldx, 1 - x, \
                    ly if (end if oldy else begin) else None, oldy

        def all_turns(eng, turn):
            turn(0, True, False, True)
            with eng.Fori(1, TURNS - 1) as i:
                turn(i, True, True, True)
            turn(TURNS - 1, True, True, False)
            turn(TURNS, False, True, False)

        @block.sync
        def _(sp):
            sp.dma_start(cond[:, :], a["cond_1024"]).then_inc(cond_loaded, 16)
            sp.dma_start(consts[:, :], a["shape_consts"]).then_inc(cond_loaded, 16)
            sp.dma_start(cols[:, :], a["bias_cols"]).then_inc(cond_loaded, 16)
            sp.dma_start(rows[:, :, :].rearrange("p r d -> p (r d)"),
                         a["bias_rows"].to_broadcast([P, NROWS * D])).then_inc(cond_loaded, 16)
            for tile, ap in cond_weight_loads:
                sp.dma_start(tile[:, :, :], ap.rearrange("(t p) n -> p t n", p=P)).then_inc(cond_loaded, 16)
            for s in range(STREAMS):
                sp.dma_start(x_in[s][:, :], a["x"][s]).then_inc(xc_loaded[s], 16)
                sp.dma_start(c_in[s][:, :], a["ctx_1024"][s]).then_inc(xc_loaded[s], 16)
            for tile, ap in weight_loads:
                sp.dma_start(tile[:, :, :], ap.rearrange("(t p) n -> p t n", p=P)).then_inc(w_loaded, 16)
            sp.wait_ge(setup, ALL_SET)
            sp.dma_start(gates_dram, gates[:, :, :].rearrange("b r d -> b (r d)")).then_inc(gates_stored, 16)
            sp.wait_ge(gates_stored, 16)
            for s in range(STREAMS):
                sp.dma_start(gate[s][:, :, :].rearrange("p r d -> p (r d)"),
                             gates_dram[s:s + 1, :].to_broadcast([P, 4 * D])).then_inc(gate_loaded[s], 16)

            def turn(i, begin, end, more):
                c = Counts(sp, i)
                c16 = 16 * i if isinstance(i, int) else sp.to_reg(sp.snap(16 * i))
                for s in range(STREAMS):
                    if begin and more:
                        sp.wait_ge(tc_done[s], c.once(0))
                        sp.wait_ge(in_h_ready[s], c.once(0))
                        sp.wait_ge(xb0_ready[s], c.once(0))
                        sp.dma_start(x_in[s][:, :], sample(a["x"], i + 1, s)).then_inc(xc_loaded[s], 16)
                        sp.dma_start(c_in[s][:, :], sample(a["ctx_1024"], i + 1, s)).then_inc(xc_loaded[s], 16)
                    if end:
                        sp.wait_ge(y_ready[s], c.once(1))
                        sp.dma_start(sample(out, i - 1, s), y[s][:, :]).then_inc(y_stored[s], 16)
                        sp.wait_ge(y_stored[s], c16)
                    if begin and end:
                        sp.dma_start(gate[s][:, :, :].rearrange("p r d -> p (r d)"), gates_of(i, s))\
                            .then_inc(gate_loaded[s], 16)

            all_turns(sp, turn)

        @block.gpsimd
        def _(pool):
            for j, val in enumerate((1e-5, 1e-6, -0.5)):
                nc.gpsimd.memset(eps_pow[:, j, :], val).then_inc(modtab_ready, 1)
            for s in range(STREAMS):
                nc.gpsimd.memset(v[s][:], 0.0).then_inc(modtab_ready, 1)
                nc.gpsimd.memset(nm[s][:], 0.0).then_inc(modtab_ready, 1)
            pool.wait_ge(cond_loaded, N_COND)
            pool.wait_ge(modtab_ready, TABLES)

            def input_step(n, s, count, loaded, before, attended_before):
                pool.wait_ge(modtab_ready, TABLES)
                after(pool, t0_copied[s], before)
                nc.gpsimd.tensor_copy(in_mod[s][:, :], mod_tab[:, bass.ds(2 * n + s, 1), 0:NMOD // 2]
                                      .rearrange("p b m -> p (b m)")).then_inc(in_mod_copied[s], 1)
                pool.wait_ge(in_aggr_done[s], count)
                nc.gpsimd.tensor_tensor(in_ve[s][:, :], in_mv[s][:, :, 1], eps_pow[:, 0, :], ALU.add)\
                    .then_inc(in_ve_ready[s], 1)
                pool.wait_ge(in_ve_ready[s], count)
                nc.gpsimd.tensor_tensor(in_rstd[s][:, :], in_ve[s][:, :], eps_pow[:, 2, :], ALU.pow)\
                    .then_inc(in_rstd_ready[s], 1)
                pool.wait_ge(xc_loaded[s], loaded)
                after(pool, x_ready[s], attended_before)
                nc.gpsimd.tensor_tensor(xb0[s][:, :], x_in[s][:, :], rows[:, RP0, :], ALU.add)\
                    .then_inc(xb0_ready[s], 1)

            def norm_step(c, s, l, old, loaded):
                pool.wait_ge(ve_ready[s], c.att(l, old))
                nc.gpsimd.tensor_tensor(rstd[s][:, :], ve[s][:, :], eps_pow[:, 2, 0:1], ALU.pow)\
                    .then_inc(rstd_ready[s], 1)
                if l == 0:
                    pool.wait_ge(gate_loaded[s], loaded)
                pool.wait_ge(x_ready[s], c.att(l, old))
                bias = (gate[s][:, 1, :], rows[:, RCA, :], gate[s][:, 3, :])[l]
                nc.gpsimd.tensor_tensor(xb[s][:, :], xres[s][:, :], bias, ALU.add).then_inc(xb_ready[s], 1)

            def mod_step(c, i, s):
                pool.wait_ge(modtab_ready, TABLES)
                after(pool, t_copied[s], c.at(3, 0))
                nc.gpsimd.tensor_copy(mod[s][:, :], mod_tab[:, bass.ds(2 * i + s, 1), NMOD // 2:NMOD]
                                      .rearrange("p b m -> p (b m)")).then_inc(mod_copied[s], 1)

            def turn(i, begin, end, more):
                c = Counts(pool, i)
                fixed = isinstance(i, int)
                c16 = 16 * i + 16 if fixed else pool.to_reg(pool.snap(16 * i + 16))
                c32 = 32 * i + 32 if fixed else pool.to_reg(pool.snap(32 * i + 32))
                c64 = 32 * i + 64 if fixed else pool.to_reg(pool.snap(32 * i + 64))
                c2 = i + 2 if fixed else pool.to_reg(pool.snap(i + 2))
                for k, (x, lx, oldx, y_, ly, oldy) in enumerate(slots(begin, end)):
                    if k in (0, 3):
                        if end:
                            norm_step(c, y_, 2, 1, c16)
                    elif ly is not None:
                        norm_step(c, y_, ly - 1, oldy, c16)
                    if k in (1, 4) and begin:
                        mod_step(c, i, x)
                    if k == 1 and begin:
                        input_step(i, 1, c.once(0), c32, c.at(1, 0), c.at(3, -2))
                    if k == 4 and more:
                        input_step(i + 1, 0, c2, c64, c.at(1, 1), c.at(3, 1))

            input_step(0, 0, 1, 32, 0, 0)
            all_turns(pool, turn)

        @block.scalar
        def _(act):
            act.wait_ge(cond_loaded, N_COND)
            nc.scalar.activation(cond_e[:, :], cond[:, :], ACT.Exp, scale=-1.0).then_inc(setup, 1)
            act.wait_ge(modtab_ready, TABLES)

            def modulate(dst, src, table, scale, shift, t):
                scale, shift = scale % (NMOD // 2) + t, shift % (NMOD // 2) + t
                return nc.scalar.activation(dst[:, t, :], src, ACT.Identity, scale=table[:, scale:scale + 1],
                                            bias=table[:, shift:shift + 1])

            def inputs_copy(c, s):
                act.wait_ge(in_mod_copied[s], c.once(0))
                act.wait_ge(t0_done[s], c.once(0))
                for t in range(KT):
                    modulate(xT[s], ps_kv[:, t * P:(t + 1) * P], in_mod[s], M_SCQ, M_BQ, t)
                for t in range(KT):
                    last = modulate(cT[s], ps_kv[:, (2 + t) * P:(3 + t) * P], in_mod[s], M_SCKV, M_BKV, t)
                last.then_inc(t0_copied[s], 1)
                act.wait_ge(tc_done[s], c.once(0))
                nc.scalar.copy(crT[s][:, :, :].rearrange("p t n -> p (t n)"), ps_q[:, 0:D]).then_inc(tc_copied[s], 1)

            def transposed_copy(c, s, l, old):
                bank_t = ps_q if l == 3 else ps_kv
                act.wait_ge(t_done[s], c.att(l - 1, old))
                if l == 1:
                    act.wait_ge(mod_copied[s], c.once(old))
                for t in range(KT):
                    src = bank_t[:, t * P:(t + 1) * P]
                    if l == 1:
                        last = modulate(xT[s], src, mod[s], M_SCSA, M_SHSA, t)
                    elif l == 3:
                        last = modulate(mlpT[s], src, mod[s], M_SCFF, M_SHFF, t)
                    else:
                        last = nc.scalar.copy(xT[s][:, t, :], src)
                last.then_inc(t_copied[s], 1)

            def k_copy(c, s, l, old):
                act.wait_ge(k_done[s], c.att(l, old))
                for t in range(KT):
                    nc.scalar.activation(k32[s][:, t, :], ps_kv[:, t * P:(t + 1) * P], ACT.Identity,
                                         bias=cols[:, BK[l] + t:BK[l] + t + 1]).then_inc(k_copied[s][t], 1)

            def q_copy(c, s, l, old):
                act.wait_ge(q_done[s], c.att(l, old))
                for dst, copied in ((qr, q_rounded), (q32, q_copied)):
                    for t in range(KT):
                        last = nc.scalar.activation(dst[s][:, t, :], ps_q[:, t * P:(t + 1) * P], ACT.Identity,
                                                    bias=cols[:, BQ[l] + t:BQ[l] + t + 1])
                    last.then_inc(copied[s], 1)

            def k_mask(c, s, l, old):
                act.wait_ge(k_copied[s][1], c.att(l, old))
                for j in range(4):
                    last = nc.scalar.activation(kr[s][:, 1, j, :], k32[s][:, 1, :], ACT.Copy, scale=keymask[:, j:j + 1])
                last.then_inc(k_rounded[s][1], 1)

            def q_mask(c, s, l, old):
                act.wait_ge(q_copied[s], c.att(l, old))
                for j in range(8):
                    last = nc.scalar.activation(qm[s][:, :, j, :], q32[s][:, :, :], ACT.Copy,
                                                scale=querymask[:, j:j + 1])
                    if j % 4 == 3:
                        last.then_inc(q_masked[s][j // 4], 1)

            def exps(c, s, l, old, units):
                for u in units:
                    act.wait_ge(st_done[s][u], c.att(l, old))
                    nc.scalar.activation(prob[s][:, 4 * u:4 * u + 4, :].rearrange("p h n -> p (h n)"),
                                         ps_st[u % 2][:, :], ACT.Exp, scale=SCALE).then_inc(exp_done[s][u], 1)

            def gelu(c, s):
                for m in range(MT):
                    if m % 4 == 0:
                        act.wait_ge(fc1_done[s][m // 4], c.once(1))
                    last = nc.scalar.activation(hT[s][:, m, :], ps_s[m // 4][:, (m % 4) * P:(m % 4 + 1) * P],
                                                ACT.Gelu_apprx_tanh, bias=cols[:, FC1B + m:FC1B + m + 1])
                last.then_inc(gelu_done[s], 1)

            def turn(i, begin, end, more):
                c = Counts(act, i)
                for k, (x, lx, oldx, y_, ly, oldy) in enumerate(slots(begin, end)):
                    if k in (1, 4) and end:
                        gelu(c, x)
                    if lx is not None:
                        exps(c, x, lx, oldx, (0, 1))
                    if k in (0, 3) and begin:
                        inputs_copy(c, y_)
                    if ly is not None and k not in (0, 3):
                        transposed_copy(c, y_, ly, oldy)
                    if lx is not None:
                        exps(c, x, lx, oldx, (2, 3))
                    if ly is not None:
                        k_copy(c, y_, ly, oldy)
                        k_mask(c, y_, ly, oldy)
                        q_copy(c, y_, ly, oldy)
                    if k in (0, 3) and end:
                        transposed_copy(c, y_, 3, 1)
                    if ly is not None:
                        q_mask(c, y_, ly, oldy)

            all_turns(act, turn)

        @block.vector
        def _(dve):
            dve.wait_ge(cond_loaded, N_COND)
            nc.vector.tensor_copy(ident_b[:, :], ident)
            nc.vector.tensor_copy(sel[:, :, :], consts[:, C_SEL:C_SEL + H].unsqueeze(2).to_broadcast([P, H, P]))
            dve.wait_ge(setup, EXP_COND)
            nc.vector.tensor_scalar(cond_d[:, :], cond_e[:, :], 1.0, None, ALU.add).then_inc(setup, 1)
            dve.wait_ge(setup, COND_PLUS_1)
            nc.vector.reciprocal(cond_r[:, :], cond_d[:, :]).then_inc(setup, 1)
            dve.wait_ge(setup, COND_INVERTED)
            nc.vector.tensor_tensor(cond_s[:, :], cond[:, :], cond_r[:, :], ALU.mult).then_inc(setup, 1)
            dve.wait_ge(setup, SILU_TRANSPOSED)
            nc.vector.tensor_copy(condT[:, :, :].rearrange("p t b -> p (t b)"), bank[0][:, 0:KT * B])\
                .then_inc(setup, 1)
            dve.wait_ge(setup, MOD_PRODUCTS)
            for j in range(NMOD):
                one = 1.0 if (j - j % 2) in (M_SCQ, M_SCKV, M_SCSA, M_SCFF) else 0.0
                nc.vector.tensor_scalar(mod_tab[:, :, j], bank[1 + j // 8][:, (j % 8) * B:(j % 8 + 1) * B],
                                        cols[:, MODB + j:MODB + j + 1], one, ALU.add, ALU.add)\
                    .then_inc(modtab_ready, 1)
            for j in range(2):
                nc.vector.tensor_tensor(gates[:, 2 * j, :], bank[3][0:B, j * D:(j + 1) * D],
                                        rows[0:B, RGSA + j, :], ALU.add).then_inc(setup, 1)
            dve.wait_ge(setup, GATES_READY)
            for j in range(2):
                nc.vector.tensor_tensor(gates[:, 2 * j + 1, :], gates[:, 2 * j, :],
                                        rows[0:B, (RSA, RFC2)[j], :], ALU.mult).then_inc(setup, 1)
            dve.wait_ge(modtab_ready, TABLES)

            def input_step(s, count, loaded):
                dve.wait_ge(xc_loaded[s], loaded)
                nc.vector.bn_stats(in_stats[s][:, 0, :], x_in[s][:, :])
                nc.vector.bn_stats(in_stats[s][:, 1, :], c_in[s][:, :]).then_inc(in_stat_done[s], 1)
                dve.wait_ge(modtab_ready, TABLES)
                dve.wait_ge(in_stat_done[s], count)
                nc.vector.bn_aggr(in_mv[s][:, 0, :], in_stats[s][:, 0, :])
                nc.vector.bn_aggr(in_mv[s][:, 1, :], in_stats[s][:, 1, :]).then_inc(in_aggr_done[s], 1)

            def input_normalize(s, count):
                dve.wait_ge(in_rstd_ready[s], count)
                nc.vector.tensor_scalar(in_hn[s][:, 0, :], x_in[s][:, :], in_mv[s][:, 0, 0:1], in_rstd[s][:, 0:1],
                                        ALU.subtract, ALU.mult)
                nc.vector.tensor_scalar(in_hn[s][:, 1, :], c_in[s][:, :], in_mv[s][:, 1, 0:1], in_rstd[s][:, 1:2],
                                        ALU.subtract, ALU.mult).then_inc(in_h_ready[s], 1)

            def residual(c, s, l, old, loaded):
                dve.wait_ge(o_proj[s], c.att(l, old))
                if l == 0:
                    dve.wait_ge(xb0_ready[s], c.once(old))
                else:
                    dve.wait_ge(xb_ready[s], c.att(l - 1, old))
                src, base = ps_o[s][:, 0:D], (xb0 if l == 0 else xb)[s]
                if l == 1:
                    dve.wait_ge(gate_loaded[s], loaded)
                    nc.vector.tensor_tensor(tmp[s][:, :], src, gate[s][:, 0, :], ALU.mult).then_inc(o_gated[s], 1)
                    dve.wait_ge(o_gated[s], c.once(old))
                    src = tmp[s][:, :]
                nc.vector.tensor_tensor(xres[s][:, :], src, base[:, :], ALU.add).then_inc(x_ready[s], 1)
                dve.wait_ge(x_ready[s], c.att(l, old))
                nc.vector.bn_stats(stats[s][:, :], xres[s][:, :]).then_inc(stat_done[s], 1)
                dve.wait_ge(modtab_ready, TABLES)
                dve.wait_ge(stat_done[s], c.att(l, old))
                nc.vector.bn_aggr(mv[s][:, :], stats[s][:, :]).then_inc(aggr_done[s], 1)
                dve.wait_ge(aggr_done[s], c.att(l, old))
                nc.vector.tensor_tensor(ve[s][:, :], mv[s][:, 1:2], eps_pow[:, 1, 0:1], ALU.add).then_inc(ve_ready[s], 1)

            def normalize(c, s, l, old):
                dve.wait_ge(rstd_ready[s], c.att(l, old))
                nc.vector.tensor_scalar(hn[s][:, :], xres[s][:, :], mv[s][:, 0:1], rstd[s][:, 0:1],
                                        ALU.subtract, ALU.mult).then_inc(h_ready[s], 1)

            def k_round(c, s, l, old):
                dve.wait_ge(k_copied[s][0], c.att(l, old))
                for j in range(4):
                    last = nc.vector.tensor_scalar(kr[s][:, 0, j, :], k32[s][:, 0, :], keymask[:, j:j + 1], None,
                                                   ALU.mult)
                last.then_inc(k_rounded[s][0], 1)

            def v_copy(c, s, l, old):
                dve.wait_ge(v_done[s], c.att(l, old))
                nc.vector.tensor_tensor(v[s][:, :, 0:4:3, :],
                                        ps_kv[:, 0:D].rearrange("p (j e d) -> p j e d", e=2, d=HD),
                                        rows[:, RV[l], :].rearrange("p (j e d) -> p j e d", e=2, d=HD),
                                        ALU.add).then_inc(v_copied[s], 1)

            def row_max(c, s, l, old, u):
                dve.wait_ge(s_done[s][u], c.att(l, old))
                nc.vector.tensor_reduce(mx[s][:, 4 * u:4 * u + 4],
                                        ps_s[u % 2][:, :].rearrange("p (h k) -> p h k", h=4),
                                        AX.X, ALU.max).then_inc(max_done[s][u], 1)

            def max_split(c, s, l, old):
                for u in range(U):
                    dve.wait_ge(max_done[s][u], c.att(l, old))
                nc.vector.tensor_scalar(nm[s][:, 0:H], mx[s][:, :], -1.0, None, ALU.mult).then_inc(nm_high[s], 1)
                dve.wait_ge(nm_high[s], c.att(l, old))
                nc.vector.scalar_tensor_tensor(out=nm[s][:, H:2 * H], in0=mx[s][:, :], scalar=-1.0, in1=nm[s][:, 0:H],
                                               op0=ALU.mult, op1=ALU.subtract).then_inc(nm_ready[s], 1)

            def max_copy(c, s, l, old):
                dve.wait_ge(mt_done[s], c.att(l, old))
                nc.vector.tensor_copy(mT[s][:, :], ps_o[s][:, 0:P // 2].bitcast(BF16)).then_inc(mt_ready[s], 1)

            def invert_sums(c, s, l, old):
                dve.wait_ge(sums_done[s], c.att(l, old))
                nc.vector.reciprocal(rsum[s][:, :, :].rearrange("p t n -> p (t n)"), ps_st[0][:, 0:D])\
                    .then_inc(sum_inverted[s], 1)

            def attention_normalize(c, s, l, old):
                dve.wait_ge(av_done[s], c.att(l, old))
                dve.wait_ge(sum_inverted[s], c.att(l, old))
                nc.vector.tensor_tensor(oT[s][:, :, :].rearrange("p t n -> p (t n)"), ps_o[s][:, 0:D],
                                        rsum[s][:, :, :].rearrange("p t n -> p (t n)"), ALU.mult)\
                    .then_inc(o_ready[s], 1)

            def finish(c, s):
                dve.wait_ge(fc2_done[s], c.once(1))
                dve.wait_ge(xb_ready[s], c.att(2, 1))
                nc.vector.tensor_tensor(tmp[s][:, :], ps_s[0][:, 0:D], gate[s][:, 2, :], ALU.mult).then_inc(y_gated[s], 1)
                dve.wait_ge(y_gated[s], c.once(1))
                nc.vector.tensor_tensor(y[s][:, :], tmp[s][:, :], xb[s][:, :], ALU.add).then_inc(y_ready[s], 1)

            def turn(i, begin, end, more):
                c = Counts(dve, i)
                fixed = isinstance(i, int)
                c16 = 16 * i + 16 if fixed else dve.to_reg(dve.snap(16 * i + 16))
                c16_old = 16 * i if fixed else dve.to_reg(dve.snap(16 * i))
                c32 = 32 * i + 32 if fixed else dve.to_reg(dve.snap(32 * i + 32))
                c64 = 32 * i + 64 if fixed else dve.to_reg(dve.snap(32 * i + 64))
                c2 = i + 2 if fixed else dve.to_reg(dve.snap(i + 2))
                for k, (x, lx, oldx, y_, ly, oldy) in enumerate(slots(begin, end)):
                    before = ((2, 1) if end else None) if k in (0, 3) else (ly - 1, oldy) if ly is not None else None
                    if before:
                        residual(c, y_, *before, c16_old if before[1] else c16)
                    if lx is not None:
                        max_copy(c, x, lx, oldx)
                        v_copy(c, x, lx, oldx)
                    if before:
                        normalize(c, y_, *before)
                    if k in (1, 4) and end:
                        finish(c, x)
                    if k == 1 and begin:
                        input_step(1, c.once(0), c32)
                    if k == 2 and begin:
                        input_normalize(1, c.once(0))
                    if k == 4 and more:
                        input_step(0, c2, c64)
                    if k == 5 and more:
                        input_normalize(0, c2)
                    if ly is not None:
                        k_round(c, y_, ly, oldy)
                    if lx is not None:
                        invert_sums(c, x, lx, oldx)
                    if lx is not None:
                        attention_normalize(c, x, lx, oldx)
                    if ly is not None:
                        for u in range(U):
                            row_max(c, y_, ly, oldy, u)
                        max_split(c, y_, ly, oldy)

            input_step(0, 1, 32)
            input_normalize(0, 1)
            all_turns(dve, turn)

        @block.tensor
        def _(pe):
            pe.wait_ge(cond_loaded, N_COND)
            pe.wait_ge(setup, SILU_READY)
            for t in range(KT):
                last = nc.tensor.transpose(bank[0][:, t * B:(t + 1) * B], cond_s[:, t * P:(t + 1) * P], ident[0:B, 0:B])
            last.then_inc(setup, 1)
            pe.wait_ge(setup, SILU_COPIED)
            sources = [(w_ssq, 0), (w_ssq, 1), (w_sskv, 0), (w_sskv, 1), (w_ada, 0), (w_ada, 1), (w_ada, 3), (w_ada, 4)]
            for j in range(NMOD):
                w, part = sources[j // KT]
                c0 = part * D + (j % KT) * P
                for t in range(KT):
                    nc.tensor.matmul(bank[1 + j // 8][:, (j % 8) * B:(j % 8 + 1) * B], w[:, t, c0:c0 + P],
                                     condT[:, t, :], start=t == 0, stop=t == KT - 1)
            for j in range(2):
                for t in range(KT):
                    c0 = (2, 5)[j] * D
                    last = nc.tensor.matmul(bank[3][0:B, j * D:(j + 1) * D], condT[:, t, :], w_ada[:, t, c0:c0 + D],
                                            start=t == 0, stop=t == KT - 1)
            last.then_inc(setup, 1)
            pe.wait_ge(setup, ALL_SET)
            pe.wait_ge(modtab_ready, TABLES)
            pe.wait_ge(w_loaded, N_W)

            def transpose_inputs(c, s):
                pe.wait_ge(in_h_ready[s], c.once(0))
                for j in range(2):
                    for t in range(KT):
                        last = nc.tensor.transpose(ps_kv[:, (2 * j + t) * P:(2 * j + t + 1) * P],
                                                   in_hn[s][:, j, t * P:(t + 1) * P], ident)
                last.then_inc(t0_done[s], 1)
                for t in range(KT):
                    last = nc.tensor.transpose(ps_q[:, t * P:(t + 1) * P], c_in[s][:, t * P:(t + 1) * P], ident)
                last.then_inc(tc_done[s], 1)

            def transpose_x(c, s, l, old):
                pe.wait_ge(h_ready[s], c.att(l - 1, old))
                bank_t = ps_q if l == 3 else ps_kv
                for t in range(KT):
                    last = nc.tensor.transpose(bank_t[:, t * P:(t + 1) * P], hn[s][:, t * P:(t + 1) * P], ident)
                last.then_inc(t_done[s], 1)

            def project_k(c, s, l, old):
                src = (cT, xT, crT)[l][s]
                for m in range(KT):
                    for t in range(KT):
                        last = nc.tensor.matmul(ps_kv[:, m * P:(m + 1) * P], w_k[l][:, t, m * P:(m + 1) * P],
                                                src[:, t, :], start=t == 0, stop=t == KT - 1)
                last.then_inc(k_done[s], 1)

            def project_q(c, s, l, old):
                for m in range(KT):
                    for t in range(KT):
                        last = nc.tensor.matmul(ps_q[:, m * P:(m + 1) * P], w_q[l][:, t, m * P:(m + 1) * P],
                                                xT[s][:, t, :], start=t == 0, stop=t == KT - 1)
                last.then_inc(q_done[s], 1)

            def project_v(c, s, l, old):
                for t in range(KT):
                    pe.wait_ge(k_copied[s][t], c.att(l, old))
                src = (cT, xT, crT)[l][s]
                for t in range(KT):
                    last = nc.tensor.matmul(ps_kv[:, 0:D], src[:, t, :], w_v[l][:, t, :],
                                            start=t == 0, stop=t == KT - 1)
                last.then_inc(v_done[s], 1)

            def scores(c, s, l, old, u):
                pe.wait_ge(k_rounded[s][u // 2], c.att(l, old))
                pe.wait_ge(q_rounded[s], c.att(l, old))
                if u >= 2:
                    pe.wait_ge(max_done[s][u - 2], c.att(l, old))
                r = slice(64 * (u % 2), 64 * (u % 2) + 64)
                nc.tensor.matmul(ps_s[u % 2][:, :], qr[s][r, u // 2, :], kr[s][r, u // 2, :, :],
                                 start=True, stop=True).then_inc(s_done[s][u], 1)

            def transpose_max(c, s, l, old):
                pe.wait_ge(nm_ready[s], c.att(l, old))
                nc.tensor.transpose(ps_o[s][:, 0:P // 2].bitcast(BF16), nm[s][:, :],
                                    ident_b[:, :]).then_inc(mt_done[s], 1)

            def scores_transposed(c, s, l, old, u):
                pe.wait_ge(q_masked[s][u % 2], c.att(l, old))
                if u >= 2:
                    pe.wait_ge(exp_done[s][u - 2], c.att(l, old))
                j0 = 4 * (u % 2)
                nc.tensor.matmul(ps_st[u % 2][:, :], k32[s][:, u // 2, :], qm[s][:, u // 2, j0:j0 + 4, :],
                                 start=True, stop=False)

            def subtract_max(c, s, l, old, u):
                pe.wait_ge(mt_ready[s], c.att(l, old))
                for j in range(4):
                    last = nc.tensor.matmul(ps_st[u % 2][:, j * P:(j + 1) * P], sel[:, 4 * u + j, :], mT[s][:, :],
                                            start=False, stop=j == 3)
                last.then_inc(st_done[s][u], 1)

            def attend(c, s, l, old, t):
                pe.wait_ge(exp_done[s][2 * t + 1], c.att(l, old))
                if t == 0:
                    pe.wait_ge(v_copied[s], c.att(l, old))
                for e in range(2):
                    for g in range(G):
                        last = nc.tensor.matmul(ps_o[s][32 * g:32 * g + 32, t * P:(t + 1) * P],
                                         v[s][:, 4 * t + g, 2 * e:2 * e + 2, :], prob[s][:, 8 * t + 2 * g + e, :],
                                         start=e == 0, stop=e == 1)

                if t == KT - 1:
                    last.then_inc(av_done[s], 1)

            def sums(c, s, l, old):
                pe.wait_ge(exp_done[s][3], c.att(l, old))
                for e in range(2):
                    for g in range(G):
                        last = nc.tensor.matmul(ps_st[0][32 * g:32 * g + 32, 0:D], ones_of[:, e, :],
                                                prob[s][:, 2 * g + e::8, :], start=e == 0, stop=e == 1)
                last.then_inc(sums_done[s], 1)

            def project_out(c, s, l, old):
                pe.wait_ge(o_ready[s], c.att(l, old))
                for t in range(KT):
                    last = nc.tensor.matmul(ps_o[s][:, 0:D], oT[s][:, t, :], w_o[l][:, t, :],
                                            start=t == 0, stop=t == KT - 1)
                last.then_inc(o_proj[s], 1)

            def fc1(c, s):
                pe.wait_ge(t_copied[s], c.att(2, 1))
                for m in range(MT):
                    for t in range(KT):
                        last = nc.tensor.matmul(ps_s[m // 4][:, (m % 4) * P:(m % 4 + 1) * P],
                                                w_fc1[:, t, m * P:(m + 1) * P], mlpT[s][:, t, :],
                                                start=t == 0, stop=t == KT - 1)
                    if m % 4 == 3:
                        last.then_inc(fc1_done[s][m // 4], 1)

            def fc2(c, s):
                pe.wait_ge(gelu_done[s], c.once(1))
                for m in range(MT):
                    last = nc.tensor.matmul(ps_s[0][:, 0:D], hT[s][:, m, :], w_fc2[:, m, :],
                                            start=m == 0, stop=m == MT - 1)
                last.then_inc(fc2_done[s], 1)

            def turn(i, begin, end, more):
                c = Counts(pe, i)
                for k, (x, lx, oldx, y_, ly, oldy) in enumerate(slots(begin, end)):
                    X = (c, x, lx, oldx)
                    Y = (c, y_, ly, oldy)
                    attends, projects = lx is not None, ly is not None
                    edge = k in (0, 3)
                    mlp = k in (1, 4) and end
                    if edge and end:
                        project_out(c, y_, 2, 1)
                    elif projects and not edge:
                        project_out(c, y_, ly - 1, oldy)
                    if mlp:
                        bank_s_free(c, k, begin)
                        fc1(c, x)
                    if attends:
                        scores_transposed(*X, 0)
                        transpose_max(*X)
                        scores_transposed(*X, 1)
                        subtract_max(*X, 0)
                    if edge and begin:
                        bank_kv_free(c, k, begin)
                        transpose_inputs(c, y_)
                    if attends:
                        subtract_max(*X, 1)
                    if mlp:
                        fc2(c, x)
                    if projects and not edge:
                        bank_kv_free(c, k, begin)
                        transpose_x(c, y_, ly, oldy)
                    if attends:
                        scores_transposed(*X, 2)
                        subtract_max(*X, 2)
                        scores_transposed(*X, 3)
                        subtract_max(*X, 3)
                    if projects:
                        if edge:
                            pe.wait_ge(t0_copied[y_], c.once(0))
                            pe.wait_ge(tc_copied[y_], c.once(0))
                        else:
                            pe.wait_ge(t_copied[y_], c.att(ly - 1, oldy))
                        project_k(*Y)
                    if attends:
                        sums(*X)
                    if projects:
                        project_q(*Y)
                    if attends:
                        attend(*X, 0)
                        attend(*X, 1)
                    if projects:
                        bank_s_free(c, k, begin)
                        if mlp:
                            pe.wait_ge(y_gated[x], c.once(1))
                        scores(*Y, 0)
                        scores(*Y, 1)
                    if edge and end:
                        if begin:
                            pe.wait_ge(q_copied[y_], c.att(0, 0))
                        transpose_x(c, y_, 3, 1)
                    if projects:
                        project_v(*Y)
                        scores(*Y, 2)
                        scores(*Y, 3)

            def last_projection(c, k, begin):
                if not begin:
                    return 1, c.at(3, -1 if k < 2 else 0)
                return [(1, c.at(3, -1)), (0, c.at(3, 1)), (1, c.at(3, 0)), (0, c.at(3, 2)), (1, c.at(3, 1)),
                        (0, c.at(3, 3))][k]

            def bank_kv_free(c, k, begin):
                s, count = last_projection(c, k, begin)
                after(pe, v_copied[s], count)

            def bank_s_free(c, k, begin):
                s, count = last_projection(c, k, begin)
                for u in (2, 3):
                    after(pe, max_done[s][u], count)

            all_turns(pe, turn)


def shape_constants():
    import numpy as np
    c = np.zeros((P, NCONST), np.float32)
    p = np.arange(P)
    c[:, C_ID:C_ID + P] = np.eye(P)
    for j in range(4):
        c[:, C_HEADMASK + j] = (p // HD) % 4 == j
    for j in range(8):
        c[:, C_HEADMASK + 4 + j] = p // HD == j
    for e in range(2):
        c[:, C_ONES + 32 * e + HD * e:C_ONES + 32 * e + HD * (e + 1)] = 1
    for h in range(H):
        c[:, C_SEL + h] = (p < 2 * H) & (p % H == h)
    return c


def kernel(**inputs):
    import numpy as np
    import concourse.bacc as bacc
    from concourse.bass_utils import run_bass_kernel_spmd

    nc = bacc.Bacc("TRN2", target_bir_lowering=False, num_devices=1)
    arrays, aps = {}, {}

    def give(name, value):
        value = np.ascontiguousarray(value)
        arrays[f"in_{name}"] = value
        aps[name] = nc.dram_tensor(f"in_{name}", value.shape, mybir.dt.from_np(value.dtype), kind="ExternalInput").ap()

    matrices = ["x", "ctx_1024", "cond_1024"] + ["L0_xcond_" + n for n in ("Wq", "Wkv", "Wp", "Wss_q", "Wss_kv")]
    matrices += ["L1_xcond_" + n for n in ("adaln_w", "qkv_w", "sa_proj_w", "q_w", "kv_w", "ca_proj_w", "fc1_w", "fc2_w")]
    for name in matrices:
        give(name, inputs[name])
    v = {n: np.asarray(a) for n, a in inputs.items() if np.ndim(a) == 1}
    bkv0, qkvb, kvb = v["L0_xcond_bkv"], v["L1_xcond_qkv_b"], v["L1_xcond_kv_b"]
    ssq, sskv, ada = v["L0_xcond_bss_q"], v["L0_xcond_bss_kv"], v["L1_xcond_adaln_b"]
    by_dim = [v["L0_xcond_bq"], qkvb[0:D], v["L1_xcond_q_b"], bkv0[0:D], qkvb[D:2 * D], kvb[0:D],
              ssq, sskv, ada[0:2 * D], ada[3 * D:5 * D], v["L1_xcond_fc1_b"]]
    give("bias_cols", np.concatenate(by_dim).reshape(-1, P).T)
    by_token = [bkv0[D:], qkvb[2 * D:], kvb[D:], v["L0_xcond_bp"], v["L1_xcond_sa_proj_b"], v["L1_xcond_ca_proj_b"],
                v["L1_xcond_fc2_b"], ada[2 * D:3 * D], ada[5 * D:6 * D]]
    give("bias_rows", np.concatenate(by_token)[None])
    give("shape_consts", shape_constants())
    out = nc.dram_tensor("out_x", (B, P, D), F32, kind="ExternalOutput").ap()
    build(nc, aps, out)
    r = run_bass_kernel_spmd(nc, [arrays], core_ids=[0])
    return r.results[0]["out_x"]
```
